# Optimizing a Trainium2 kernel written in Bass

```python
import numpy as np
import jax
import jax.numpy as jnp

def _softmax(x, axis=-1):
    return jax.nn.softmax(x, axis=axis)

def _gelu(x):
    return jax.nn.gelu(x, approximate=True)

def _silu(x):
    return jax.nn.silu(x)

def _sigmoid(x):
    return jax.nn.sigmoid(x)

def _layernorm(x, axis=-1, eps=1e-05):
    m = jnp.mean(x, axis=axis, keepdims=True)
    v = jnp.var(x, axis=axis, keepdims=True)
    return (x - m) / jnp.sqrt(v + eps)

def _scatter_add(tgt, idx, src, axis=0):
    return tgt.at[idx].add(src)

def _segment_sum(src, seg, n):
    return jax.ops.segment_sum(src, seg, n)
kernel_name = 'mk_dlrm_tower_d1_rec_r8_bcf40b'

def setup_inputs(seed: int=0):
    np.random.seed(seed)
    _w = jnp.asarray

    def _rec_inputs():
        import jax
        import jax.numpy as jnp
        _tk = jax.random.key(seed)
        ids = jnp.stack([jax.random.randint(jax.random.fold_in(_tk, 200 + f), (2048,), 0, v, jnp.int32) for f, v in enumerate([1000, 125000, 1250, 12500, 1250, 12500, 1000, 1000, 1000, 1000, 12500, 1250, 1250, 1000, 12500, 1000, 12500, 12500, 1000, 1250, 1000, 1000, 1000, 1250, 1000, 12500])], axis=1)
        tbl_0 = 0.05 * jax.random.normal(jax.random.fold_in(_tk, 500 + 0), (1000, 128), jnp.float32)
        tbl_1 = 0.05 * jax.random.normal(jax.random.fold_in(_tk, 500 + 1), (125000, 128), jnp.float32)
        tbl_2 = 0.05 * jax.random.normal(jax.random.fold_in(_tk, 500 + 2), (1250, 128), jnp.float32)
        tbl_3 = 0.05 * jax.random.normal(jax.random.fold_in(_tk, 500 + 3), (12500, 128), jnp.float32)
        tbl_4 = 0.05 * jax.random.normal(jax.random.fold_in(_tk, 500 + 4), (1250, 128), jnp.float32)
        tbl_5 = 0.05 * jax.random.normal(jax.random.fold_in(_tk, 500 + 5), (12500, 128), jnp.float32)
        tbl_6 = 0.05 * jax.random.normal(jax.random.fold_in(_tk, 500 + 6), (1000, 128), jnp.float32)
        tbl_7 = 0.05 * jax.random.normal(jax.random.fold_in(_tk, 500 + 7), (1000, 128), jnp.float32)
        tbl_8 = 0.05 * jax.random.normal(jax.random.fold_in(_tk, 500 + 8), (1000, 128), jnp.float32)
        tbl_9 = 0.05 * jax.random.normal(jax.random.fold_in(_tk, 500 + 9), (1000, 128), jnp.float32)
        tbl_10 = 0.05 * jax.random.normal(jax.random.fold_in(_tk, 500 + 10), (12500, 128), jnp.float32)
        tbl_11 = 0.05 * jax.random.normal(jax.random.fold_in(_tk, 500 + 11), (1250, 128), jnp.float32)
        tbl_12 = 0.05 * jax.random.normal(jax.random.fold_in(_tk, 500 + 12), (1250, 128), jnp.float32)
        tbl_13 = 0.05 * jax.random.normal(jax.random.fold_in(_tk, 500 + 13), (1000, 128), jnp.float32)
        tbl_14 = 0.05 * jax.random.normal(jax.random.fold_in(_tk, 500 + 14), (12500, 128), jnp.float32)
        tbl_15 = 0.05 * jax.random.normal(jax.random.fold_in(_tk, 500 + 15), (1000, 128), jnp.float32)
        tbl_16 = 0.05 * jax.random.normal(jax.random.fold_in(_tk, 500 + 16), (12500, 128), jnp.float32)
        tbl_17 = 0.05 * jax.random.normal(jax.random.fold_in(_tk, 500 + 17), (12500, 128), jnp.float32)
        tbl_18 = 0.05 * jax.random.normal(jax.random.fold_in(_tk, 500 + 18), (1000, 128), jnp.float32)
        tbl_19 = 0.05 * jax.random.normal(jax.random.fold_in(_tk, 500 + 19), (1250, 128), jnp.float32)
        tbl_20 = 0.05 * jax.random.normal(jax.random.fold_in(_tk, 500 + 20), (1000, 128), jnp.float32)
        tbl_21 = 0.05 * jax.random.normal(jax.random.fold_in(_tk, 500 + 21), (1000, 128), jnp.float32)
        tbl_22 = 0.05 * jax.random.normal(jax.random.fold_in(_tk, 500 + 22), (1000, 128), jnp.float32)
        tbl_23 = 0.05 * jax.random.normal(jax.random.fold_in(_tk, 500 + 23), (1250, 128), jnp.float32)
        tbl_24 = 0.05 * jax.random.normal(jax.random.fold_in(_tk, 500 + 24), (1000, 128), jnp.float32)
        tbl_25 = 0.05 * jax.random.normal(jax.random.fold_in(_tk, 500 + 25), (12500, 128), jnp.float32)
        _rk = jax.random.fold_in(_tk, 7)
        r_dense = -0.000520686 + 1.00062 * jax.random.normal(jax.random.fold_in(_rk, 101), (2048, 128), jnp.float32)
        W_top1 = 0.0456912 * jax.random.normal(jax.random.fold_in(_tk, 801), (479, 512), jnp.float32)
        W_top2 = 0.0441942 * jax.random.normal(jax.random.fold_in(_tk, 802), (512, 256), jnp.float32)
        W_top3 = 0.0625 * jax.random.normal(jax.random.fold_in(_tk, 803), (256, 1), jnp.float32)
        b_top1 = jnp.zeros((512,), jnp.float32)
        b_top2 = jnp.zeros((256,), jnp.float32)
        return (r_dense, ids, tbl_0, tbl_1, tbl_2, tbl_3, tbl_4, tbl_5, tbl_6, tbl_7, tbl_8, tbl_9, tbl_10, tbl_11, tbl_12, tbl_13, tbl_14, tbl_15, tbl_16, tbl_17, tbl_18, tbl_19, tbl_20, tbl_21, tbl_22, tbl_23, tbl_24, tbl_25, W_top1, b_top1, W_top2, b_top2, W_top3)
    r_dense, ids, tbl_0, tbl_1, tbl_2, tbl_3, tbl_4, tbl_5, tbl_6, tbl_7, tbl_8, tbl_9, tbl_10, tbl_11, tbl_12, tbl_13, tbl_14, tbl_15, tbl_16, tbl_17, tbl_18, tbl_19, tbl_20, tbl_21, tbl_22, tbl_23, tbl_24, tbl_25, W_top1, b_top1, W_top2, b_top2, W_top3 = _rec_inputs()

    def _L0_rec_setup():
        import jax, jax.numpy as jnp
        import numpy as np
        B, NUM_EMBS, D = (2048, 26, 128)
        key = jax.random.key(seed)
        k1, k2 = jax.random.split(key)
        dense = jax.random.normal(k1, (B, D), dtype=jnp.float32)
        embs = jax.random.normal(k2, (B, NUM_EMBS, D), dtype=jnp.float32)
        return {'dense': dense, 'embs': embs}
    _L0_rec_all = _L0_rec_setup()
    _L0_rec_in = {k: v for k, v in _L0_rec_all.items() if k in ()}
    del _L0_rec_all
    return {'r_dense': r_dense, 'ids': ids, 'tbl_0': tbl_0, 'tbl_1': tbl_1, 'tbl_2': tbl_2, 'tbl_3': tbl_3, 'tbl_4': tbl_4, 'tbl_5': tbl_5, 'tbl_6': tbl_6, 'tbl_7': tbl_7, 'tbl_8': tbl_8, 'tbl_9': tbl_9, 'tbl_10': tbl_10, 'tbl_11': tbl_11, 'tbl_12': tbl_12, 'tbl_13': tbl_13, 'tbl_14': tbl_14, 'tbl_15': tbl_15, 'tbl_16': tbl_16, 'tbl_17': tbl_17, 'tbl_18': tbl_18, 'tbl_19': tbl_19, 'tbl_20': tbl_20, 'tbl_21': tbl_21, 'tbl_22': tbl_22, 'tbl_23': tbl_23, 'tbl_24': tbl_24, 'tbl_25': tbl_25, 'W_top1': W_top1, 'b_top1': b_top1, 'W_top2': W_top2, 'b_top2': b_top2, 'W_top3': W_top3}

def reference(r_dense, ids, tbl_0, tbl_1, tbl_2, tbl_3, tbl_4, tbl_5, tbl_6, tbl_7, tbl_8, tbl_9, tbl_10, tbl_11, tbl_12, tbl_13, tbl_14, tbl_15, tbl_16, tbl_17, tbl_18, tbl_19, tbl_20, tbl_21, tbl_22, tbl_23, tbl_24, tbl_25, W_top1, b_top1, W_top2, b_top2, W_top3):
    import jax
    import jax.numpy as jnp

    def _L0_rec_ref(dense, embs):
        import jax, jax.numpy as jnp
        import numpy as np
        B, NUM_EMBS, D = (2048, 26, 128)
        T = jnp.concatenate([dense[:, None, :], embs], axis=1)
        N = T.shape[1]
        Z = jnp.einsum('bnd,bmd->bnm', T, T)
        iu0, iu1 = jnp.triu_indices(N, k=1)
        return Z[:, iu0, iu1]
    e = jnp.stack([tbl_0[ids[:, 0]], tbl_1[ids[:, 1]], tbl_2[ids[:, 2]], tbl_3[ids[:, 3]], tbl_4[ids[:, 4]], tbl_5[ids[:, 5]], tbl_6[ids[:, 6]], tbl_7[ids[:, 7]], tbl_8[ids[:, 8]], tbl_9[ids[:, 9]], tbl_10[ids[:, 10]], tbl_11[ids[:, 11]], tbl_12[ids[:, 12]], tbl_13[ids[:, 13]], tbl_14[ids[:, 14]], tbl_15[ids[:, 15]], tbl_16[ids[:, 16]], tbl_17[ids[:, 17]], tbl_18[ids[:, 18]], tbl_19[ids[:, 19]], tbl_20[ids[:, 20]], tbl_21[ids[:, 21]], tbl_22[ids[:, 22]], tbl_23[ids[:, 23]], tbl_24[ids[:, 24]], tbl_25[ids[:, 25]]], axis=1)
    z = _L0_rec_ref(r_dense, e)
    z = z.reshape(z.shape[0], -1)
    h = jnp.concatenate([z, r_dense], axis=1)
    h = jnp.maximum(h @ W_top1 + b_top1, 0.0)
    h = jnp.maximum(h @ W_top2 + b_top2, 0.0)
    y = h @ W_top3
    return y

_drawn_inputs = setup_inputs


def setup_inputs(seed=0):
    import zlib

    import numpy as np

    out = dict(_drawn_inputs(seed))
    spreads = {'b_top1': (0.0, 0.1), 'b_top2': (0.0, 0.1)}
    factors = {}
    for name, (base, spread) in spreads.items():
        noise = np.random.default_rng([zlib.crc32(name.encode()), seed]).standard_normal(out[name].shape)
        drawn = base * np.exp(spread * noise) if base else spread * noise
        out[name] = jnp.asarray(drawn.astype(out[name].dtype))
    for name, factor in factors.items():
        out[name] = (out[name] * factor).astype(out[name].dtype)
    return out
```

```python
from contextlib import ExitStack

import concourse.bass as bass
from concourse import mybir

F32 = mybir.dt.float32
I32 = mybir.dt.int32
U32 = mybir.dt.uint32
ALU = mybir.AluOpType
ACT = mybir.ActivationFunctionType

P = 128
QUAD = 32
GROUP = P // QUAD
TILES = 2
FPB = 4
UNIT = 8
GPB = 4


def dlrm_tower(nc, dense, ids, tables, w1, b1, w2, b2, w3, out):
    B, _ = dense.shape
    NEMB = len(tables)
    NF = NEMB + 1
    H1, H2 = w1.shape[1], w2.shape[1]
    PASSES = B // (P * TILES)
    NS = P * TILES
    TGROUPS = -(-NF // FPB)
    UNITS = P // (GROUP * UNIT)
    ZC = -(-(NF - 1) // GROUP)
    ZQ_LAST = (NF - 1) - GROUP * (ZC - 1)
    C1, O1, O2 = ZC + 1, H1 // P, H2 // P
    PAIRS = NF * (NF - 1) // 2

    ids_t = ids.rearrange("(t p) f -> t p f", p=P)
    dense_t = dense.rearrange("(t p) d -> t p d", p=P)

    with ExitStack() as ctx:
        def sb(name, shape, dt=F32):
            return ctx.enter_context(nc.sbuf_tensor(name, shape, dt))

        def psum(name, shape):
            return ctx.enter_context(nc.psum_tensor(name, shape, F32))

        def sem(name):
            return ctx.enter_context(nc.semaphore(name))

        idx = sb("idx", [P, TILES, NEMB], I32)
        emb = sb("emb", [P, TILES, NF, P])
        xt = sb("xt", [P, TILES, P, QUAD])
        zs = sb("zs", [P, C1, NS])
        ident = sb("ident", [P, P])
        w1s = sb("w1s", [P, C1, H1])
        w2s = sb("w2s", [P, O1, H2])
        w3s = sb("w3s", [P, O2])
        b1s = sb("b1s", [P, O1])
        b2s = sb("b2s", [P, O2])
        h1 = sb("h1", [P, O1, NS])
        h2 = sb("h2", [P, O2, NS])
        yrow = sb("yrow", [1, B])

        turned = [psum(f"turned{e}", [P, FPB, P]) for e in range(2)]
        zps = [psum(f"zps{e}", [P, UNIT // GPB, 512]) for e in range(2)]
        hps = [psum(f"hps{e}", [P, 2, NS]) for e in range(2)]

        ident_zero = sem("ident_zero")
        ident_ready = sem("ident_ready")
        w1_zero = sem("w1_zero")
        weights_ready = sem("weights_ready")
        pad_ready = sem("pad_ready")
        idx_ready = [sem(f"idx_ready{k}") for k in range(TILES)]
        dense_ready = [sem(f"dense_ready{k}") for k in range(TILES)]
        tile_opened = sem("tile_opened")
        gathered = [[sem(f"gathered{k}_{g}") for g in range(TGROUPS)] for k in range(TILES)]
        emb_free = [sem(f"emb_free{k}") for k in range(TILES)]
        turned_full = [sem(f"turned_full{e}") for e in range(2)]
        turned_taken = [sem(f"turned_taken{e}") for e in range(2)]
        z_full = [sem(f"z_full{e}") for e in range(2)]
        z_taken = [sem(f"z_taken{e}") for e in range(2)]
        h1_full = [sem(f"h1_full{e}") for e in range(2)]
        h1_taken = [sem(f"h1_taken{e}") for e in range(2)]
        h2_full = sem("h2_full")
        h2_taken = sem("h2_taken")
        y_full = sem("y_full")
        y_taken = sem("y_taken")
        out_written = sem("out_written")

        def bank_of(k, g):
            return (k * TGROUPS + g) % 2, (k * TGROUPS + g) // 2

        TURNS = [(TILES * TGROUPS + 1 - e) // 2 for e in range(2)]
        ZU = TILES * UNITS // 2

        def features(g):
            return range(g * FPB, min(NF, (g + 1) * FPB))

        block = ctx.enter_context(nc.Block())

        @block.sync
        def _(sp):
            with sp.Fori(0, PASSES) as i:
                for k in range(TILES):
                    sp.wait_ge(emb_free[k], i + 1)
                    sp.dma_start(idx[:, k, :], ids_t[bass.ds(TILES * i + k, 1), :, :].rearrange("a p f -> p (a f)")
                                 ).then_inc(idx_ready[k], 16)
                    sp.dma_start(emb[:, k, 0, :], dense_t[bass.ds(TILES * i + k, 1), :, :].rearrange("a p d -> p (a d)")
                                 ).then_inc(dense_ready[k], 16)
            sp.wait_ge(y_taken, PASSES)
            sp.dma_start(out.rearrange("b a -> a b"), yrow[:]).then_inc(out_written, 16)
            sp.wait_ge(out_written, 16)

        @block.gpsimd
        def _(pool):
            nc.gpsimd.memset(ident[:], 0.0).then_inc(ident_zero, 1)
            pool.wait_ge(ident_zero, 1)
            nc.gpsimd.affine_select(out=ident[:], in_=ident[:], compare_op=ALU.not_equal, fill=1.0, base=0,
                                    pattern=[[-1, P]], channel_multiplier=1).then_inc(ident_ready, 1)
            with pool.Fori(0, PASSES) as i:
                for k in range(TILES):
                    pool.wait_ge(idx_ready[k], 16 * i + 16)
                    pool.sem_inc(tile_opened, 1)
                    for g in range(TGROUPS):
                        for f in features(g):
                            if f == 0:
                                continue
                            pool.indirect_dma_start(
                                emb[:, k, f, :], None, tables[f - 1],
                                bass.IndirectOffsetOnAxis(ap=idx[:, k, f - 1:f].bitcast(U32), axis=0),
                            ).then_inc(gathered[k][g], 16)

        def load_weights(act):
            act.wait_ge(w1_zero, 1)
            row = 0
            for m in range(1, NF):
                c, q = (m - 1) // GROUP, (m - 1) % GROUP
                act.dma_start(w1s[QUAD * q:QUAD * q + m, c, :], w1[row:row + m, :]).then_inc(weights_ready, 16)
                row += m
            act.dma_start(w1s[:, ZC, :], w1[PAIRS:PAIRS + P, :]).then_inc(weights_ready, 16)
            act.dma_start(w2s[:], w2.rearrange("(c p) n -> p c n", p=P)).then_inc(weights_ready, 16)
            act.dma_start(w3s[:], w3).then_inc(weights_ready, 16)
            act.dma_start(b1s[:], b1).then_inc(weights_ready, 16)
            act.dma_start(b2s[:], b2).then_inc(weights_ready, 16)

        WEIGHT_DMAS = (NF - 1) + 5

        def take_turned(eng, copy, e, i, k):
            for g in range(TGROUPS):
                reader, nth = bank_of(k, g)
                if reader != e:
                    continue
                fs = features(g)
                eng.wait_ge(turned_full[e], TURNS[e] * i + nth + 1)
                if g == 0:
                    copy(zs[:, ZC, k * P:(k + 1) * P], turned[e][:, 0, :])
                copy(xt[:, k, :, fs[0]:fs[-1] + 1],
                     turned[e][:, 0:len(fs), :].rearrange("p f s -> p s f")).then_inc(turned_taken[e], 1)

        def take_z(eng, copy, e, i, k):
            for u in range(e, UNITS, 2):
                nth = (k * UNITS + u) // 2
                eng.wait_ge(z_full[e], ZU * i + nth + 1)
                for j in range(GROUP):
                    blocks = zps[e][QUAD * j:QUAD * (j + 1), :, 0:GPB * GROUP * NF].rearrange(
                        "p b (g c) -> p b g c", g=GPB)
                    for q in range(GROUP):
                        nch = ZC if q < ZQ_LAST else ZC - 1
                        c0 = j * NF + 1 + q
                        s0 = k * P + u * UNIT * GROUP + j
                        for b in range(UNIT // GPB):
                            o0 = s0 + b * GPB * GROUP
                            last = copy(
                                zs[QUAD * q:QUAD * (q + 1), 0:nch, o0:o0 + GPB * GROUP - j:GROUP]
                                .rearrange("p c g -> p g c"),
                                blocks[:, b, :, c0:c0 + GROUP * (nch - 1) + 1:GROUP])
                last.then_inc(z_taken[e], 1)

        @block.vector
        def _(dve):
            nc.vector.memset(w1s[:], 0.0).then_inc(w1_zero, 1)
            nc.vector.memset(xt[:], 0.0).then_inc(pad_ready, 1)
            dve.wait_ge(pad_ready, 1)
            for s in (turned_taken[0], z_taken[0]):
                dve.sem_inc(s, 1)
            dve.wait_ge(weights_ready, 16 * WEIGHT_DMAS)
            with dve.Fori(0, PASSES) as i:
                for k in range(TILES):
                    take_turned(dve, nc.vector.tensor_copy, 0, i, k)
                    take_z(dve, nc.vector.tensor_copy, 0, i, k)
                dve.wait_ge(h1_full[0], i + 1)
                for o in range(O1 // 2):
                    last = nc.vector.tensor_scalar(h1[:, o, :], hps[0][:, o, :], b1s[:, o:o + 1], 0.0,
                                                   ALU.add, ALU.max)
                last.then_inc(h1_taken[0], 1)
                dve.wait_ge(h2_full, i + 1)
                for o in range(O2):
                    last = nc.vector.tensor_scalar(h2[:, o, :], hps[0][:, o, :], b2s[:, o:o + 1], 0.0,
                                                   ALU.add, ALU.max)
                last.then_inc(h2_taken, 1)

        @block.scalar
        def _(act):
            load_weights(act)
            act.wait_ge(pad_ready, 1)
            for s in (turned_taken[1], z_taken[1]):
                act.sem_inc(s, 1)
            act.wait_ge(weights_ready, 16 * WEIGHT_DMAS)
            with act.Fori(0, PASSES) as i:
                for k in range(TILES):
                    take_turned(act, nc.scalar.copy, 1, i, k)
                    take_z(act, nc.scalar.copy, 1, i, k)
                act.wait_ge(h1_full[1], i + 1)
                for o in range(O1 // 2):
                    last = nc.scalar.activation(h1[:, O1 // 2 + o, :], hps[1][:, o, :], ACT.Relu,
                                                bias=b1s[:, O1 // 2 + o:O1 // 2 + o + 1])
                last.then_inc(h1_taken[1], 1)
                act.wait_ge(y_full, i + 1)
                nc.scalar.copy(yrow[:, bass.ds(i * NS, NS)], hps[1][0:1, 0, :]).then_inc(y_taken, 1)

        @block.tensor
        def _(pe):
            pe.wait_ge(ident_ready, 1)
            for k in range(TILES):
                pe.sem_inc(emb_free[k], 1)
            pe.wait_ge(weights_ready, 16 * WEIGHT_DMAS)

            def turn(i, k):
                for g in range(TGROUPS):
                    e, nth = bank_of(k, g)
                    pe.wait_ge(turned_taken[e], TURNS[e] * i + nth + 1)
                    if g == 0:
                        pe.wait_ge(dense_ready[k], 16 * i + 16)
                    n = len([f for f in features(g) if f > 0])
                    pe.wait_ge(gathered[k][g], 16 * n * i + 16 * n)
                    for x, f in enumerate(features(g)):
                        last = nc.tensor.transpose(turned[e][:, x, :], emb[:, k, f, :], ident[:])
                    last.then_inc(turned_full[e], 1)

            def products(i, k):
                for e in range(2):
                    n = len([g for kk in range(k + 1) for g in range(TGROUPS) if bank_of(kk, g)[0] == e])
                    pe.wait_ge(turned_taken[e], TURNS[e] * i + n + 1)
                pe.sem_inc(emb_free[k], 1)
                for u in range(UNITS):
                    e, nth = u % 2, (k * UNITS + u) // 2
                    pe.wait_ge(z_taken[e], ZU * i + nth + 1)
                    for g in range(UNIT):
                        s = (u * UNIT + g) * GROUP
                        last = nc.tensor.matmul(
                            zps[e][:, g // GPB, (g % GPB) * GROUP * NF:(g % GPB + 1) * GROUP * NF],
                            xt[:, k, s:s + GROUP, :].rearrange("p s f -> p (s f)"),
                            xt[:, k, s:s + GROUP, 0:NF], start=True, stop=True)
                    last.then_inc(z_full[e], 1)

            with pe.Fori(0, PASSES) as i:
                for k in range(TILES):
                    turn(i, k)
                    products(i, k)
                for e in range(2):
                    pe.wait_ge(z_taken[e], ZU * i + ZU + 1)
                for o in range(O1):
                    e = o // (O1 // 2)
                    for c in range(C1):
                        kk = QUAD * ZQ_LAST if c == ZC - 1 else P
                        last = nc.tensor.matmul(hps[e][:, o % (O1 // 2), :], w1s[0:kk, c, o * P:(o + 1) * P],
                                                zs[0:kk, c, :], start=(c == 0), stop=(c == C1 - 1))
                    if o % (O1 // 2) == O1 // 2 - 1:
                        last.then_inc(h1_full[e], 1)
                for e in range(2):
                    pe.wait_ge(h1_taken[e], i + 1)
                for o in range(O2):
                    for c in range(O1):
                        last = nc.tensor.matmul(hps[0][:, o, :], w2s[:, c, o * P:(o + 1) * P], h1[:, c, :],
                                                start=(c == 0), stop=(c == O1 - 1))
                last.then_inc(h2_full, 1)
                pe.wait_ge(h2_taken, i + 1)
                for c in range(O2):
                    last = nc.tensor.matmul(hps[1][0:1, 0, :], w3s[:, c:c + 1], h2[:, c, :],
                                            start=(c == 0), stop=(c == O2 - 1))
                last.then_inc(y_full, 1)
                pe.wait_ge(y_taken, i + 1)


def kernel(**inputs):
    import numpy as np
    import concourse.bacc as bacc
    from concourse.bass_utils import run_bass_kernel_spmd

    nc = bacc.Bacc("TRN2", target_bir_lowering=False, num_devices=1)
    arrays = {}

    def dram(name, a):
        arrays[name] = np.ascontiguousarray(a)
        return nc.dram_tensor(name, arrays[name].shape, mybir.dt.from_np(arrays[name].dtype),
                              kind="ExternalInput").ap()

    ids = inputs["ids"]
    n = ids.shape[1] + 1
    first = [a * n - a * (a + 1) // 2 - a - 1 for a in range(n)]
    order = [first[a] + m for m in range(1, n) for a in range(m)]
    w1 = np.asarray(inputs["W_top1"])
    order = order + list(range(len(order), w1.shape[0]))
    args = dict(
        dense=dram("dense", inputs["r_dense"]), ids=dram("ids", ids),
        tables=[dram(f"tbl_{f}", inputs[f"tbl_{f}"]) for f in range(n - 1)],
        w1=dram("w1", w1[np.array(order)]),
        b1=dram("b1", np.asarray(inputs["b_top1"]).reshape(-1, P).T),
        w2=dram("w2", inputs["W_top2"]),
        b2=dram("b2", np.asarray(inputs["b_top2"]).reshape(-1, P).T),
        w3=dram("w3", np.asarray(inputs["W_top3"]).reshape(-1, P).T),
    )
    out = nc.dram_tensor("scores", (ids.shape[0], 1), F32, kind="ExternalOutput").ap()
    dlrm_tower(nc, out=out, **args)
    r = run_bass_kernel_spmd(nc, [arrays], core_ids=[0])
    return r.results[0]["scores"]
```

```python
from contextlib import ExitStack

import concourse.bass as bass
from concourse import mybir

F32 = mybir.dt.float32
F32R = mybir.dt.float32r
BF16 = mybir.dt.bfloat16
I32 = mybir.dt.int32
U32 = mybir.dt.uint32
ALU = mybir.AluOpType
ACT = mybir.ActivationFunctionType

P = 128
LOG_P = 7
QUAD = 32
GROUP = P // QUAD
TILES = 2
FPB = 4
UNIT = 8
RING = 3
STAGE = 8 * P

TABLED = [6, 7, 8, 9, 20, 21, 22]


def feature_order(nemb):
    return [0] + [1 + f for f in range(nemb) if f not in TABLED] + [1 + f for f in TABLED]


def dlrm_tower(nc, dense, ids, tables, w1, w2, b2, w3, out):
    B = dense.shape[0]
    NEMB = len(tables)
    NF = NEMB + 1
    order = feature_order(NEMB)
    NT = len(TABLED)
    NG = NF - NT
    H1, H2 = w1.shape[2], w2.shape[1]
    PASSES = B // (P * TILES)
    NS = P * TILES
    TG = -(-NG // FPB)
    UNITS = P // (GROUP * UNIT)
    SHIFTS = (NF - 1) // 2
    ZC = 3
    ZR = NF * SHIFTS // ZC
    C1, O1, O2 = ZC + 1, H1 // P, H2 // P
    QS = NS // GROUP
    GT = P // GROUP
    TC = STAGE // P
    ROWS = [tables[f].shape[0] for f in TABLED]

    ids_t = ids.rearrange("(t p) f -> t p f", p=P)
    dense_t = dense.rearrange("(t p) d -> t p d", p=P)
    out_row = out.rearrange("b a -> a b")

    MLP = {1: ("l1", 0), 3: ("l1", 1), 4: ("l2",), 5: ("l3",)}
    LAG = 2

    def fills(mlp):
        o = [("turn", 0, g) for g in range(TG)]
        for t in range(NT):
            o += [("look", t)] + ([MLP[t]] if mlp and t in MLP else [])
        return o + [("turn", 1, g) for g in range(TG)]

    FIRST, STEADY, LAST = fills(False), fills(True), list(MLP.values())
    assert len(STEADY) % RING == 0

    def fill_number(i, what):
        if isinstance(i, int) and i < LAG:
            return len(FIRST) * i + FIRST.index(what)
        if isinstance(i, int) and i >= PASSES:
            return len(FIRST) * LAG + len(STEADY) * (PASSES - LAG) + len(LAST) * (i - PASSES) + LAST.index(what)
        return (i - LAG) * len(STEADY) + len(FIRST) * LAG + STEADY.index(what)

    def bank(i, what):
        if isinstance(i, int):
            return fill_number(i, what) % RING
        return (len(FIRST) * LAG + STEADY.index(what)) % RING

    with ExitStack() as ctx:
        def sb(name, shape, dt=F32):
            return ctx.enter_context(nc.sbuf_tensor(name, shape, dt))

        def psum(name, shape):
            return ctx.enter_context(nc.psum_tensor(name, shape, F32))

        def sem(name):
            return ctx.enter_context(nc.semaphore(name))

        idx = sb("idx", [P, TILES, NEMB], I32)
        emb = sb("emb", [P, TILES, NG, P])
        xt = sb("xt", [P, TILES, P, QUAD])
        ident = sb("ident", [P, P])
        row_of_int = sb("row_of_int", [P, TC], I32)
        row_of = sb("row_of", [P, TC])
        pick = sb("pick", [2 * NT, NT, P], BF16)
        ids_turned = sb("ids_turned", [2 * NT, B], BF16)
        table = sb("table", [P, NT, 2, TC, P], F32R)
        onehot = sb("onehot", [P, 2, TC, NS], F32R)
        zb = sb("zb", [P, NF, QS])
        zs = sb("zs", [P, C1, NS])
        zs_hi = sb("zs_hi", [P, C1, NS], F32R)
        zs_lo = sb("zs_lo", [P, C1, NS], F32R)
        w1_hi = sb("w1_hi", [P, C1, H1], F32R)
        w1_lo = sb("w1_lo", [P, C1, H1], F32R)
        w2_hi = sb("w2_hi", [P, O1, H2], F32R)
        w2_lo = sb("w2_lo", [P, O1, H2], F32R)
        w3s = sb("w3s", [P, O2])
        b2s = sb("b2s", [P, O2])
        h1_hi = sb("h1_hi", [P, O1, NS], F32R)
        h1_lo = sb("h1_lo", [P, O1, NS], F32R)
        h2 = sb("h2", [P, O2, NS])
        yrow = sb("yrow", [1, NS])

        ring = [psum(f"ring{r}", [P, 512]) for r in range(RING)]
        idb = psum("idb", [P, 2, NS])
        zps = [psum(f"zps{e}", [P, UNIT, P]) for e in range(2)]

        bounce = nc.dram_tensor("bounce", (GROUP, QUAD, NF + SHIFTS, QS), F32, kind="Internal").ap()

        scratch = xt[:, 1, :, :].rearrange("p s f -> p (s f)")
        NB_T = B // P
        ids_all = scratch[:, 0:NB_T * NEMB].bitcast(I32).rearrange("p (t f) -> p t f", f=NEMB)
        at = NB_T * NEMB
        halves_int = scratch[:, at:at + NB_T * 2 * NT].bitcast(I32).rearrange("p (t h) -> p t h", h=2 * NT)
        at += NB_T * 2 * NT
        halves = scratch[:, at:at + NB_T * 2 * NT].rearrange("p (t h) -> p t h", h=2 * NT)

        stage = [zs[:, :, :].rearrange("p c s -> p (c s)"), zb[:, :, :].rearrange("p m s -> p (m s)")[:, 0:STAGE]]
        WPC = STAGE // H1
        PIECES = [("table", t) for t in range(NT)] + [("w2", 0)] + [("w1", c) for c in range(0, C1, WPC)]

        consts_zero = sem("consts_zero")
        consts_made = sem("consts_made")
        stage_zero = sem("stage_zero")
        stage_loaded = [sem(f"stage_loaded{h}") for h in range(2)]
        piece_hi = sem("piece_hi")
        piece_lo = sem("piece_lo")
        small_loaded = sem("small_loaded")
        ids_loaded = sem("ids_loaded")
        halves_step = sem("halves_step")
        ids_turned_full = sem("ids_turned_full")
        ids_turned_taken = sem("ids_turned_taken")
        xt_padded = sem("xt_padded")
        bias_step = sem("bias_step")
        idx_ready = [sem(f"idx_ready{k}") for k in range(TILES)]
        dense_ready = [sem(f"dense_ready{k}") for k in range(TILES)]
        tile_opened = sem("tile_opened")
        gathered = [[sem(f"gathered{k}_{g}") for g in range(TG)] for k in range(TILES)]
        ring_full = sem("ring_full")
        ring_taken = sem("ring_taken")
        idb_opened = sem("idb_opened")
        idb_full = sem("idb_full")
        onehot_made = sem("onehot_made")
        z_full = [sem(f"z_full{e}") for e in range(2)]
        z_taken = [sem(f"z_taken{e}") for e in range(2)]
        sp_passed = sem("sp_passed")
        bounce_written = sem("bounce_written")
        bounce_read = sem("bounce_read")
        dense_copied = sem("dense_copied")
        zs_hi_made = sem("zs_hi_made")
        zs_lo_made = sem("zs_lo_made")
        h1_hi_made = sem("h1_hi_made")
        h1_lo_made = sem("h1_lo_made")
        y_made = sem("y_made")
        y_written = sem("y_written")

        READ = []
        for shift in range(1, SHIFTS + 1):
            at = (shift - 1) * NF
            cuts = sorted({0, NF} | {c * ZR - at for c in range(ZC) if 0 < c * ZR - at < NF})
            READ += [(shift, a, b, (at + a) % ZR, (at + a) // ZR) for a, b in zip(cuts, cuts[1:])]
        READS = len(READ)

        def i_is(i, n):
            return isinstance(i, int) and i == n

        def turned(g):
            return range(g * FPB, min(NG, (g + 1) * FPB))

        PAIR_FILLS = -(-NT // 2)
        ZU = TILES * UNITS // 2

        def last_before(t):
            return max(x for x in range(NT) if x % 2 == t % 2)

        block = ctx.enter_context(nc.Block())

        @block.sync
        def _(sp):
            def load_tile(i, k):
                t = TILES * i + k
                sp.dma_start(idx[:, k, :], ids_t[bass.ds(t, 1), :, :].rearrange("a p f -> p (a f)")
                             ).then_inc(idx_ready[k], 16)
                sp.dma_start(emb[:, k, 0, :], dense_t[bass.ds(t, 1), :, :].rearrange("a p d -> p (a d)")
                             ).then_inc(dense_ready[k], 16)

            for k in range(TILES):
                load_tile(0, k)
            sp.dma_start(ids_all, ids.rearrange("(t p) f -> p t f", p=P)).then_inc(ids_loaded, 16)

            sp.dma_start(w3s[:], w3).then_inc(small_loaded, 16)
            sp.dma_start(b2s[:], b2).then_inc(small_loaded, 16)

            for n, (kind, x) in enumerate(PIECES):
                sp.wait_ge(stage_zero, 2)
                if n >= 2:
                    sp.wait_ge(piece_lo, n - 1)
                loaded = stage_loaded[n % 2]
                if kind == "table":
                    full = ROWS[x] // P
                    view = stage[n % 2].rearrange("p (c d) -> p c d", d=P)
                    sp.dma_start(view[:, 0:full, :], tables[TABLED[x]][0:full * P, :].rearrange("(c p) d -> p c d", p=P)
                                 ).then_inc(loaded, 16)
                    if ROWS[x] > full * P:
                        sp.dma_start(view[0:ROWS[x] - full * P, full, :], tables[TABLED[x]][full * P:ROWS[x], :]
                                     ).then_inc(loaded, 16)
                elif kind == "w2":
                    sp.dma_start(stage[n % 2].rearrange("p (c o) -> p c o", o=H2), w2.rearrange("(c p) o -> p c o", p=P)
                                 ).then_inc(loaded, 16)
                else:
                    sp.dma_start(stage[n % 2].rearrange("p (c o) -> p c o", o=H1), w1[:, x:x + WPC, :]
                                 ).then_inc(loaded, 16)

            def bounce_out(i):
                for e in range(2):
                    sp.wait_ge(z_taken[e], ZU * i + ZU)
                    sp.sem_inc(sp_passed, 1)
                if not (isinstance(i, int) and i == 0):
                    sp.wait_ge(bounce_read, 16 * READS * i)
                    sp.sem_inc(sp_passed, 1)
                rows = bounce.rearrange("j n m s -> (j n) m s")
                sp.dma_start(rows[:, 0:NF, :], zb[:]).then_inc(bounce_written, 16)
                sp.dma_start(rows[:, NF:NF + SHIFTS, :], zb[:, 0:SHIFTS, :]).then_inc(bounce_written, 16)

            def bounce_in(i):
                sp.wait_ge(bounce_written, 32 * i + 32)
                sp.sem_inc(sp_passed, 1)
                if isinstance(i, int) and i == 0:
                    sp.wait_ge(bias_step, 1)
                else:
                    sp.wait_ge(zs_lo_made, i)
                flat = bounce.rearrange("j n m s -> j (n m s)")
                step = (NF + SHIFTS + 1) * QS
                for shift, n0, n1, row, chunk in READ:
                    diagonal = flat[:, shift * QS:shift * QS + NF * step].rearrange("j (n x) -> n j x", x=step)
                    sp.dma_start(zs[row:row + n1 - n0, chunk, :].rearrange("n (j s) -> n j s", s=QS),
                                 diagonal[n0:n1, :, 0:QS]).then_inc(bounce_read, 16)

            def next_tile(i, k):
                sp.wait_ge(ring_full, fill_number(i, ("turn", k, TG - 1)) + 1)
                sp.sem_inc(sp_passed, 1)
                load_tile(i + 1, k)

            def one_pass(i):
                bounce_out(i - 1)
                next_tile(i, 0)
                bounce_in(i - 1)
                next_tile(i, 1)

            next_tile(0, 0)
            next_tile(0, 1)
            one_pass(1)
            with sp.Fori(LAG, PASSES - 1) as i:
                one_pass(i)
            for i in (PASSES - 2, PASSES - 1):
                bounce_out(i)
                bounce_in(i)
            sp.wait_ge(bounce_read, 16 * READS * PASSES)

        def piece_dmas(kind, x):
            return 2 if kind == "table" and ROWS[x] % P else 1

        def piece_loaded(n):
            return 16 * sum(piece_dmas(*PIECES[x]) for x in range(n % 2, n + 1, 2))

        def piece_split(kind, x):
            if kind == "table":
                return [table[:, x, h, :, :].rearrange("p c d -> p (c d)") for h in range(2)]
            if kind == "w2":
                return [w[:, :, :].rearrange("p c o -> p (c o)") for w in (w2_hi, w2_lo)]
            return [w[:, x:x + WPC, :].rearrange("p c o -> p (c o)") for w in (w1_hi, w1_lo)]

        @block.gpsimd
        def _(pool):
            def gather_tile(i, k):
                pool.wait_ge(idx_ready[k], 16 * i + 16)
                pool.sem_inc(tile_opened, 1)
                for g in range(TG):
                    for x in turned(g):
                        if x == 0:
                            continue
                        f = order[x] - 1
                        pool.indirect_dma_start(
                            emb[:, k, x, :], None, tables[f],
                            bass.IndirectOffsetOnAxis(ap=idx[:, k, f:f + 1].bitcast(U32), axis=0),
                        ).then_inc(gathered[k][g], 16)

            nc.gpsimd.memset(ident[:], 0.0).then_inc(consts_zero, 1)
            nc.gpsimd.memset(pick[:], 0.0).then_inc(consts_zero, 1)
            nc.gpsimd.iota(row_of_int[:], pattern=[[P, TC]], base=0, channel_multiplier=1).then_inc(consts_made, 1)
            pool.wait_ge(consts_zero, 2)
            nc.gpsimd.affine_select(out=ident[:], in_=ident[:], compare_op=ALU.not_equal, fill=1.0, base=0,
                                    pattern=[[-1, P]], channel_multiplier=1).then_inc(consts_made, 1)
            nc.gpsimd.affine_select(out=pick[:], in_=pick[:], compare_op=ALU.not_equal, fill=float(P), base=0,
                                    pattern=[[-1, NT], [0, P]], channel_multiplier=1).then_inc(consts_zero, 1)
            pool.wait_ge(consts_zero, 3)
            nc.gpsimd.affine_select(out=pick[:], in_=pick[:], compare_op=ALU.not_equal, fill=1.0, base=-NT,
                                    pattern=[[-1, NT], [0, P]], channel_multiplier=1).then_inc(consts_made, 1)
            for k in range(TILES):
                gather_tile(0, k)
            with pool.Fori(1, PASSES) as i:
                for k in range(TILES):
                    gather_tile(i, k)

        def take_z(eng, copy, e, i, k, u):
            if k == 0 and u == e and not (isinstance(i, int) and i == 0):
                eng.wait_ge(bounce_written, 32 * i)
            eng.wait_ge(z_full[e], ZU * i + (k * UNITS + u) // 2 + 1)
            s0 = k * GT + u * UNIT
            for j in range(GROUP):
                last = copy(zb[QUAD * j:QUAD * (j + 1), :, s0:s0 + UNIT],
                            zps[e][QUAD * j:QUAD * (j + 1), :, j * NF:(j + 1) * NF].rearrange("p g m -> p m g"))
            last.then_inc(z_taken[e], 1)

        @block.vector
        def _(dve):
            def make_onehot(i, t):
                dve.wait_ge(idb_full, PAIR_FILLS * i + t // 2 + 1)
                if t >= 2:
                    dve.wait_ge(ring_full, fill_number(i, ("look", t - 2)) + 1)
                elif not (isinstance(i, int) and i == 0):
                    dve.wait_ge(ring_full, fill_number(i - 1, ("look", last_before(t))) + 1)
                nc.vector.tensor_tensor(
                    onehot[:, t % 2, :, :],
                    idb[:, t % 2, :].unsqueeze(1).to_broadcast([P, TC, NS]),
                    row_of[:].unsqueeze(2).to_broadcast([P, TC, NS]),
                    ALU.is_equal).then_inc(onehot_made, 1)

            def split_h1(i, x):
                n = 2 * (i - LAG) + x + 1
                dve.wait_ge(h1_hi_made, n)
                nc.vector.scalar_tensor_tensor(
                    out=h1_lo[:, 2 * x:2 * x + 2, :].rearrange("p o s -> p (o s)"), in0=ring[bank(i, ("l1", x))][:],
                    scalar=0.0, in1=h1_hi[:, 2 * x:2 * x + 2, :].rearrange("p o s -> p (o s)").bitcast(F32),
                    op0=ALU.max, op1=ALU.subtract).then_inc(h1_lo_made, 1)

            def split_zs(i):
                dve.wait_ge(zs_hi_made, i)
                nc.vector.tensor_tensor(zs_lo[:], zs[:], zs_hi[:].bitcast(F32), ALU.subtract).then_inc(zs_lo_made, 1)

            def piece_to_lo(n):
                hi, lo = piece_split(*PIECES[n])
                dve.wait_ge(piece_hi, n + 1)
                nc.vector.tensor_tensor(lo, stage[n % 2], hi.bitcast(F32), ALU.subtract).then_inc(piece_lo, 1)

            def one_pass(i, mlp, last):
                for t in range(2, NT):
                    make_onehot(i, t)
                    if mlp and t - 1 in MLP and MLP[t - 1][0] == "l1":
                        split_h1(i, MLP[t - 1][1])
                    if i_is(i, 0) and NT + t - 2 < len(PIECES):
                        piece_to_lo(NT + t - 2)
                if i_is(i, 0):
                    dve.wait_ge(piece_lo, len(PIECES))
                    nc.vector.memset(zs[:], 1.0).then_inc(bias_step, 1)
                if not last:
                    make_onehot(i + 1, 0)
                    make_onehot(i + 1, 1)
                if not i_is(i, 0):
                    split_zs(i)
                for k in range(TILES):
                    for u in range(0, UNITS, 2):
                        take_z(dve, nc.vector.tensor_copy, 0, i, k, u)

            for piece in stage:
                nc.vector.memset(piece, 0.0).then_inc(stage_zero, 1)
            dve.wait_ge(ids_loaded, 16)
            for n, f in enumerate(TABLED):
                nc.vector.tensor_scalar(halves_int[:, :, n], ids_all[:, :, f], LOG_P, None,
                                        ALU.logical_shift_right).then_inc(halves_step, 1)
                nc.vector.tensor_scalar(halves_int[:, :, NT + n], ids_all[:, :, f], P - 1, None,
                                        ALU.bitwise_and).then_inc(halves_step, 1)
            dve.wait_ge(halves_step, 2 * NT)
            nc.vector.tensor_copy(halves, halves_int).then_inc(halves_step, 1)
            dve.wait_ge(consts_made, 3)
            nc.vector.tensor_copy(row_of[:], row_of_int[:]).then_inc(halves_step, 1)
            dve.wait_ge(halves_step, 2 * NT + 2)
            for n in range(NT):
                piece_to_lo(n)
                if n == 1:
                    make_onehot(0, 0)
                    make_onehot(0, 1)
            dve.wait_ge(ids_turned_taken, 2)
            nc.vector.memset(xt[:, :, :, NF:QUAD], 0.0).then_inc(xt_padded, 1)
            one_pass(0, mlp=False, last=False)
            one_pass(1, mlp=False, last=False)
            with dve.Fori(LAG, PASSES - 1) as i:
                one_pass(i, mlp=True, last=False)
            one_pass(PASSES - 1, mlp=True, last=True)
            for x in range(2):
                split_h1(PASSES, x)
            split_zs(PASSES)
            for x in range(2):
                split_h1(PASSES + 1, x)

        @block.scalar
        def _(act):
            def take_turn(i, k, g):
                what = ("turn", k, g)
                fs = turned(g)
                act.wait_ge(ring_full, fill_number(i, what) + 1)
                nc.scalar.copy(xt[:, k, :, fs[0]:fs[-1] + 1],
                               ring[bank(i, what)][:, 0:len(fs) * P].rearrange("p (f s) -> p s f", f=len(fs))
                               ).then_inc(ring_taken, 1)

            def take_look(i, t):
                what = ("look", t)
                act.wait_ge(ring_full, fill_number(i, what) + 1)
                nc.scalar.copy(xt[:, :, :, NG + t],
                               ring[bank(i, what)][:, 0:NS].rearrange("p (k s) -> p k s", k=TILES)
                               ).then_inc(ring_taken, 1)

            def take_l1(i, x):
                what = ("l1", x)
                act.wait_ge(ring_full, fill_number(i, what) + 1)
                nc.scalar.activation(h1_hi[:, 2 * x:2 * x + 2, :].rearrange("p o s -> p (o s)"),
                                     ring[bank(i, what)][:], ACT.Relu).then_inc(h1_hi_made, 1)
                act.wait_ge(h1_lo_made, 2 * (i - LAG) + x + 1)
                act.sem_inc(ring_taken, 1)

            def take_l2(i):
                what = ("l2",)
                act.wait_ge(ring_full, fill_number(i, what) + 1)
                for o in range(O2):
                    last = nc.scalar.activation(h2[:, o, :], ring[bank(i, what)][:, o * NS:(o + 1) * NS], ACT.Relu,
                                                bias=b2s[:, o:o + 1])
                last.then_inc(ring_taken, 1)

            def take_l3(i):
                what = ("l3",)
                act.wait_ge(ring_full, fill_number(i, what) + 1)
                n = i - LAG
                if not i_is(n, 0):
                    act.wait_ge(y_written, 16 * n)
                nc.scalar.copy(yrow[:].rearrange("o (k g j) -> o j k g", k=TILES, j=GROUP),
                               ring[bank(i, what)][0:1, 0:NS].rearrange("o (j k g) -> o j k g", k=TILES, j=GROUP)
                               ).then_inc(ring_taken, 1)
                act.wait_ge(ring_taken, fill_number(i, what) + 1)
                act.dma_start(out_row[:, bass.ds(NS * n, NS)], yrow[:]).then_inc(y_written, 16)

            def split_zs(i):
                act.wait_ge(bounce_read, 16 * READS * i)
                act.wait_ge(dense_copied, TILES * i)
                nc.scalar.copy(zs_hi[:], zs[:]).then_inc(zs_hi_made, 1)

            def piece_to_hi(n):
                act.wait_ge(stage_loaded[n % 2], piece_loaded(n))
                nc.scalar.copy(piece_split(*PIECES[n])[0], stage[n % 2]).then_inc(piece_hi, 1)

            def take_mlp(i, what):
                if what[0] == "l1":
                    take_l1(i, what[1])
                elif what[0] == "l2":
                    take_l2(i)
                else:
                    take_l3(i)

            def one_pass(i, mlp):
                for g in range(TG):
                    take_turn(i, 0, g)
                for t in range(NT):
                    take_look(i, t)
                    if mlp and t in MLP:
                        take_mlp(i, MLP[t])
                    if i_is(i, 0) and NT + t < len(PIECES):
                        piece_to_hi(NT + t)
                for g in range(TG):
                    take_turn(i, 1, g)
                if i_is(i, 0):
                    act.wait_ge(bias_step, 1)
                else:
                    split_zs(i)
                    act.wait_ge(zs_lo_made, i)
                act.wait_ge(ring_taken, fill_number(i, ("turn", 1, TG - 1)) + 1)
                for k in range(TILES):
                    nc.scalar.copy(zs[:, ZC, :].rearrange("p (j k g) -> p k j g", j=GROUP, k=TILES)[:, k],
                                   xt[:, k, :, 0].rearrange("p (g j) -> p j g", j=GROUP)).then_inc(dense_copied, 1)
                for k in range(TILES):
                    for u in range(1, UNITS, 2):
                        take_z(act, nc.scalar.copy, 1, i, k, u)

            act.wait_ge(ids_turned_full, 1)
            for e in range(2):
                w = UNIT * P
                nc.scalar.copy(ids_turned[:, e * w:(e + 1) * w], zps[e][0:2 * NT, :, :].rearrange("p t s -> p (t s)")
                               ).then_inc(ids_turned_taken, 1)
            for n in range(NT):
                piece_to_hi(n)
            act.wait_ge(small_loaded, 32)
            act.wait_ge(xt_padded, 1)

            one_pass(0, mlp=False)
            one_pass(1, mlp=False)
            with act.Fori(LAG, PASSES) as i:
                one_pass(i, mlp=True)
            for what in LAST:
                take_mlp(PASSES, what)
            split_zs(PASSES)
            for what in LAST:
                take_mlp(PASSES + 1, what)
            act.wait_ge(y_written, 16 * PASSES)

        @block.tensor
        def _(pe):
            def open_bank(i, what):
                n = fill_number(i, what)
                if not isinstance(n, int) or n >= RING:
                    pe.wait_ge(ring_taken, n - RING + 1)
                return ring[bank(i, what)]

            def turn(i, k, g):
                ps = open_bank(i, ("turn", k, g))
                n = len([x for x in turned(g) if x > 0])
                pe.wait_ge(gathered[k][g], 16 * n * i + 16 * n)
                if g == 0:
                    pe.wait_ge(dense_ready[k], 16 * i + 16)
                for x, f in enumerate(turned(g)):
                    last = nc.tensor.transpose(ps[:, x * P:(x + 1) * P], emb[:, k, f, :], ident[:])
                last.then_inc(ring_full, 1)

            def broadcast_ids(i, pair):
                done = NT * i + 2 * pair
                if not isinstance(done, int) or done > 0:
                    pe.wait_ge(onehot_made, done)
                    pe.sem_inc(idb_opened, 1)
                for t in range(2 * pair, min(NT, 2 * pair + 2)):
                    last = nc.tensor.matmul(idb[:, t % 2, :], pick[:, t, :], ids_turned[:, bass.ds(i * NS, NS)],
                                            start=True, stop=True)
                last.then_inc(idb_full, 1)

            def look_up(i, t):
                ps = open_bank(i, ("look", t))
                pe.wait_ge(onehot_made, NT * i + t + 1)
                for c in range(TC):
                    kk = min(P, ROWS[t] - c * P)
                    for h in range(2):
                        last = nc.tensor.matmul(ps[:, 0:NS], table[0:kk, t, h, c, :], onehot[0:kk, t % 2, c, :],
                                                start=(c == 0 and h == 0), stop=(c == TC - 1 and h == 1))
                last.then_inc(ring_full, 1)

            def products(i, k, u):
                e, nth = u % 2, (k * UNITS + u) // 2
                if not (isinstance(i, int) and i == 0 and nth == 0):
                    pe.wait_ge(z_taken[e], ZU * i + nth)
                for g in range(UNIT):
                    s = (u * UNIT + g) * GROUP
                    last = nc.tensor.matmul(
                        zps[e][:, g, 0:GROUP * NF],
                        xt[:, k, s:s + GROUP, :].rearrange("p s f -> p (s f)"),
                        xt[:, k, s:s + GROUP, 0:NF], start=True, stop=True)
                last.then_inc(z_full[e], 1)

            def split_product(ps, w_hi, w_lo, x_hi, x_lo, first, last_one):
                nc.tensor.matmul(ps, w_hi, x_hi, start=first, stop=False)
                nc.tensor.matmul(ps, w_hi, x_lo, start=False, stop=False)
                return nc.tensor.matmul(ps, w_lo, x_hi, start=False, stop=last_one)

            def layer1(i, x):
                ps = open_bank(i, ("l1", x))
                pe.wait_ge(zs_lo_made, i - LAG + 1)
                for o in range(2 * x, 2 * x + 2):
                    for c in range(C1):
                        kk = ZR + 1 if c == 0 else ZR if c < ZC else P
                        cols = slice(o * P, (o + 1) * P)
                        last = split_product(ps[:, (o % 2) * NS:(o % 2 + 1) * NS], w1_hi[0:kk, c, cols],
                                             w1_lo[0:kk, c, cols], zs_hi[0:kk, c, :], zs_lo[0:kk, c, :],
                                             c == 0, c == C1 - 1)
                last.then_inc(ring_full, 1)

            def layer2(i):
                ps = open_bank(i, ("l2",))
                pe.wait_ge(h1_lo_made, 2 * (i - LAG) + 2)
                for o in range(O2):
                    for c in range(O1):
                        cols = slice(o * P, (o + 1) * P)
                        last = split_product(ps[:, o * NS:(o + 1) * NS], w2_hi[:, c, cols], w2_lo[:, c, cols],
                                             h1_hi[:, c, :], h1_lo[:, c, :], c == 0, c == O1 - 1)
                last.then_inc(ring_full, 1)

            def layer3(i):
                ps = open_bank(i, ("l3",))
                pe.wait_ge(ring_taken, fill_number(i, ("l2",)) + 1)
                for c in range(O2):
                    last = nc.tensor.matmul(ps[0:1, 0:NS], w3s[:, c:c + 1], h2[:, c, :],
                                            start=(c == 0), stop=(c == O2 - 1))
                last.then_inc(ring_full, 1)

            def layer(i, what):
                if what[0] == "l1":
                    layer1(i, what[1])
                elif what[0] == "l2":
                    layer2(i)
                else:
                    layer3(i)

            def one_pass(i, mlp, last):
                for g in range(TG):
                    turn(i, 0, g)
                for t in range(NT):
                    if t % 2 == 1 and t + 1 < NT:
                        broadcast_ids(i, (t + 1) // 2)
                    look_up(i, t)
                    if mlp and t in MLP:
                        layer(i, MLP[t])
                if not last:
                    broadcast_ids(i + 1, 0)
                for g in range(TG):
                    turn(i, 1, g)
                pe.wait_ge(ring_taken, fill_number(i, ("turn", 1, TG - 1)) + 1)
                for k in range(TILES):
                    for u in range(UNITS):
                        products(i, k, u)

            pe.wait_ge(consts_made, 3)
            pe.wait_ge(halves_step, 2 * NT + 2)
            for t in range(NB_T):
                last = nc.tensor.transpose(zps[t // UNIT][0:2 * NT, t % UNIT, :], halves[:, t, :], ident[:])
            last.then_inc(ids_turned_full, 1)
            pe.wait_ge(ids_turned_taken, 2)
            broadcast_ids(0, 0)

            one_pass(0, mlp=False, last=False)
            one_pass(1, mlp=False, last=False)
            with pe.Fori(LAG, PASSES - 1) as i:
                one_pass(i, mlp=True, last=False)
            one_pass(PASSES - 1, mlp=True, last=True)
            for i in (PASSES, PASSES + 1):
                for what in LAST:
                    layer(i, what)


def kernel(**inputs):
    import numpy as np
    import concourse.bacc as bacc
    from concourse.bass_utils import run_bass_kernel_spmd

    nc = bacc.Bacc("TRN2", target_bir_lowering=False, num_devices=1)
    arrays = {}

    def dram(name, a):
        arrays[name] = np.ascontiguousarray(a)
        return nc.dram_tensor(name, arrays[name].shape, mybir.dt.from_np(arrays[name].dtype),
                              kind="ExternalInput").ap()

    ids = inputs["ids"]
    n = ids.shape[1] + 1
    order = feature_order(n - 1)
    w1 = np.asarray(inputs["W_top1"])
    pairs = n * (n - 1) // 2
    chunks = 3
    per = pairs // chunks
    w1_chunks = np.zeros((P, chunks + 1, w1.shape[1]), w1.dtype)
    for row in range(pairs):
        shift, a = row // n + 1, row % n
        b = (a + shift) % n
        lo, hi = min(order[a], order[b]), max(order[a], order[b])
        w1_chunks[row % per, row // per] = w1[lo * n - lo * (lo + 1) // 2 + hi - lo - 1]
    w1_chunks[per, 0] = np.asarray(inputs["b_top1"])
    w1_chunks[:, chunks] = w1[pairs:]
    args = dict(
        dense=dram("dense", inputs["r_dense"]), ids=dram("ids", ids),
        tables=[dram(f"tbl_{f}", inputs[f"tbl_{f}"]) for f in range(n - 1)],
        w1=dram("w1", w1_chunks),
        w2=dram("w2", inputs["W_top2"]),
        b2=dram("b2", np.asarray(inputs["b_top2"]).reshape(-1, P).T),
        w3=dram("w3", np.asarray(inputs["W_top3"]).reshape(-1, P).T),
    )
    out = nc.dram_tensor("scores", (ids.shape[0], 1), F32, kind="ExternalOutput").ap()
    dlrm_tower(nc, out=out, **args)
    r = run_bass_kernel_spmd(nc, [arrays], core_ids=[0])
    return r.results[0]["scores"]
```

```python
from contextlib import ExitStack

import concourse.bass as bass
from concourse import mybir

F32 = mybir.dt.float32
F32R = mybir.dt.float32r
BF16 = mybir.dt.bfloat16
I32 = mybir.dt.int32
U32 = mybir.dt.uint32
ALU = mybir.AluOpType
ACT = mybir.ActivationFunctionType

P = 128
LOG_P = 7
GROUP = 4
TILES = 2
FPB = 4
UNIT = 8
RING = 3
BUFS = 4
STAGE = 8 * P

TABLED = [6, 7, 8, 9, 20, 21, 22]

EARLY = [24, 0]


def feature_order(nemb):
    return [0] + [1 + f for f in range(nemb) if f not in TABLED + EARLY] + [1 + f for f in EARLY + TABLED]


def dlrm_tower(nc, dense, ids, tables, w1, w2, b2, w3, out):
    B = dense.shape[0]
    NEMB = len(tables)
    NF = NEMB + 1
    order = feature_order(NEMB)
    NT = len(TABLED)
    NE = len(EARLY)
    NG = NF - NT
    H1, H2 = w1.shape[2], w2.shape[1]
    PASSES = B // (P * TILES)
    NS = P * TILES
    TG = -(-NG // FPB)
    UNITS = P // (GROUP * UNIT)
    SHIFTS = (NF - 1) // 2
    ZC = 3
    ZR = NF * SHIFTS // ZC
    C1, O1, O2 = ZC + 1, H1 // P, H2 // P
    QS = NS // GROUP
    GT = P // GROUP
    TC = STAGE // P
    ROWS = [tables[f].shape[0] for f in TABLED + EARLY]

    ids_t = ids.rearrange("(t p) f -> t p f", p=P)
    dense_t = dense.rearrange("(t p) d -> t p d", p=P)
    out_row = out.rearrange("b a -> a b")

    LAST = [("l1", 0), ("l1", 1), ("l2",), ("l3",)]
    LAG = 2

    TURN0, TURN1 = ([("turn", k, g) for g in range(TG)] for k in range(TILES))
    LOOKS = [("look", t) for t in range(NT)]
    ALL_LOOKS = [("look", t) for t in range(NT + NE)]
    FIRST_LOOKS = 5
    OPEN = TURN0[:RING] + LOOKS[:1] + TURN0[RING:]
    FILLS = {
        "first": ALL_LOOKS[:FIRST_LOOKS] + TURN0 + ALL_LOOKS[FIRST_LOOKS:] + TURN1,
        "second": OPEN + ALL_LOOKS[1:] + TURN1,
        "steady": OPEN + LOOKS[1:BUFS] + LAST[0:1] + LOOKS[BUFS:] + TURN1 + LAST[1:],
        "last": OPEN + LOOKS[1:] + TURN1,
    }
    TAIL = [(PASSES + n, what) for n, what in (
        (-1, LAST[0]), (-1, LAST[1]), (-1, LAST[2]), (0, LAST[0]), (0, LAST[1]), (-1, LAST[3]), (0, LAST[2]),
        (1, LAST[0]), (1, LAST[1]), (0, LAST[3]), (1, LAST[2]), (1, LAST[3]))]
    assert len(FILLS["steady"]) % RING == 0

    def kind_of(i):
        return {0: "first", 1: "second", PASSES - 1: "last"}.get(i, "steady") if isinstance(i, int) else "steady"

    def fill_number(i, what):
        if isinstance(i, int) and i < LAG:
            return len(FILLS["first"]) * i + FILLS[kind_of(i)].index(what)
        before = len(FILLS["first"]) * LAG
        if isinstance(i, int) and (i, what) in TAIL:
            return before + len(FILLS["steady"]) * (PASSES - 1 - LAG) + len(FILLS["last"]) + TAIL.index((i, what))
        return (i - LAG) * len(FILLS["steady"]) + before + FILLS[kind_of(i)].index(what)

    def bank(i, what):
        if isinstance(i, int):
            return fill_number(i, what) % RING
        return (len(FILLS["first"]) * LAG + FILLS["steady"].index(what)) % RING

    with ExitStack() as ctx:
        def sb(name, shape, dt=F32):
            return ctx.enter_context(nc.sbuf_tensor(name, shape, dt))

        def psum(name, shape):
            return ctx.enter_context(nc.psum_tensor(name, shape, F32))

        def sem(name):
            return ctx.enter_context(nc.semaphore(name))

        idx = sb("idx", [P, TILES, NEMB], I32)
        emb = sb("emb", [P, TILES, NG, P])
        xt = sb("xt", [P, TILES, P, NF])
        ident = sb("ident", [P, P])
        row_of_int = sb("row_of_int", [P, TC], I32)
        row_of = sb("row_of", [P, TC])
        pick = sb("pick", [2 * (NT + NE), NT + NE], BF16)
        ids_turned = sb("ids_turned", [2 * (NT + NE), B], BF16)
        table = sb("table", [P, NT, 2, TC, P], F32R)
        onehot = sb("onehot", [P, BUFS, TC, NS], F32R)
        zb = sb("zb", [P, GROUP * NF, QS])
        zs = sb("zs", [P, C1, NS])
        zs_hi = sb("zs_hi", [P, C1, NS], F32R)
        zs_lo = sb("zs_lo", [P, C1, NS], F32R)
        w1_hi = sb("w1_hi", [P, C1, H1], F32R)
        w1_lo = sb("w1_lo", [P, C1, H1], F32R)
        w2_hi = sb("w2_hi", [P, O1, H2], F32R)
        w2_lo = sb("w2_lo", [P, O1, H2], F32R)
        w3s = sb("w3s", [P, O2])
        b2s = sb("b2s", [P, O2])
        h1_hi = sb("h1_hi", [P, O1, NS], F32R)
        h1_lo = sb("h1_lo", [P, O1, NS], F32R)
        h2 = sb("h2", [P, O2, NS])
        yrow = h2[0:1, 0, :]

        ring = [psum(f"ring{r}", [P, 512]) for r in range(RING)]
        idb = psum("idb", [P, 2, NS])
        zps = [psum(f"zps{e}", [P, UNIT, P]) for e in range(2)]

        bounce = nc.dram_tensor("bounce", (GROUP, NF + 1, NF + SHIFTS, QS), F32, kind="Internal").ap()

        flat_zb = zb[:, :, :].rearrange("p m s -> p (m s)")
        IN_ZB = GROUP * NF * QS // STAGE
        stage = [zs[:, :, :].rearrange("p c s -> p (c s)")]
        stage += [flat_zb[:, x * STAGE:(x + 1) * STAGE] for x in range(IN_ZB)]
        NB_T = B // P
        ids_all = flat_zb[:, IN_ZB * STAGE:IN_ZB * STAGE + NB_T * NEMB].bitcast(I32).rearrange(
            "p (t f) -> p t f", f=NEMB)
        NL = NT + NE
        at = IN_ZB * STAGE + NB_T * NEMB
        halves_int = flat_zb[:, at:at + NB_T * 2 * NL].bitcast(I32).rearrange("p (t h) -> p t h", h=2 * NL)
        halves = h2[:, :, :].rearrange("p o s -> p (o s)")[:, 0:NB_T * 2 * NL].rearrange("p (t h) -> p t h", h=2 * NL)
        WPC = STAGE // H1
        PIECES = [("table", t) for t in range(NL)] + [("w2", 0)] + [("w1", c) for c in range(0, C1, WPC)]
        STAGE_OF = [n % len(stage) for n in range(len(PIECES))]

        def piece_before(n):
            return max([x for x in range(n) if STAGE_OF[x] == STAGE_OF[n]], default=None)

        consts_zero = sem("consts_zero")
        consts_made = sem("consts_made")
        stage_zero = sem("stage_zero")
        stage_loaded = [sem(f"stage_loaded{h}") for h in range(len(stage))]
        piece_hi = sem("piece_hi")
        piece_lo = sem("piece_lo")
        small_loaded = sem("small_loaded")
        ids_loaded = sem("ids_loaded")
        halves_step = sem("halves_step")
        ids_turned_full = sem("ids_turned_full")
        ids_turned_taken = sem("ids_turned_taken")
        bias_step = sem("bias_step")
        idx_ready = [sem(f"idx_ready{k}") for k in range(TILES)]
        dense_ready = [sem(f"dense_ready{k}") for k in range(TILES)]
        tile_opened = sem("tile_opened")
        gathered = [[sem(f"gathered{k}_{g}") for g in range(TG)] for k in range(TILES)]
        ring_full = sem("ring_full")
        ring_taken = sem("ring_taken")
        idb_opened = sem("idb_opened")
        idb_full = sem("idb_full")
        onehot_made = sem("onehot_made")
        z_full = [sem(f"z_full{e}") for e in range(2)]
        z_taken = [sem(f"z_taken{e}") for e in range(2)]
        sp_passed = sem("sp_passed")
        bounce_written = sem("bounce_written")
        bounce_read = sem("bounce_read")
        pool_written = sem("pool_written")
        pool_read = sem("pool_read")
        dense_placed = sem("dense_placed")
        zs_hi_made = sem("zs_hi_made")
        zs_lo_made = sem("zs_lo_made")
        h1_hi_made = sem("h1_hi_made")
        h1_lo_made = sem("h1_lo_made")
        h1_opened = sem("h1_opened")
        yrow_free = sem("yrow_free")

        def i_is(i, n):
            return isinstance(i, int) and i == n

        READ = []
        for shift in range(1, SHIFTS + 1):
            at = (shift - 1) * NF
            cuts = sorted({0, NF} | {c * ZR - at for c in range(ZC) if 0 < c * ZR - at < NF})
            READ += [(shift, a, b, (at + a) % ZR, (at + a) // ZR) for a, b in zip(cuts, cuts[1:])]
        READS = len(READ)
        WRITE = [(j, 0, NF) for j in range(GROUP)] + [(j, NF, NF + SHIFTS) for j in range(GROUP)]
        WRITES = len(WRITE)
        POOL_WRITES, POOL_READS = 2, 4

        late_zs = emb[:, 0, :, :].rearrange("p f d -> p (f d)")[:, 0:C1 * NS].rearrange("p (c s) -> p c s", s=NS)

        def zs_of(i):
            return late_zs if i_is(i, PASSES - 1) else zs

        def written_before(i):
            return 16 * (WRITES * i - (POOL_WRITES if i_is(i, PASSES) else 0))

        def read_before(i):
            return 16 * (READS * i - (POOL_READS if i_is(i, PASSES) else 0))

        def write_bounce(eng, writes, done):
            for j, m0, m1 in writes:
                eng.dma_start(bounce[j, 0:NF, m0:m1, :], zb[j * NF:(j + 1) * NF, j * NF:j * NF + m1 - m0, :]
                              ).then_inc(done, 16)

        def read_bounce(eng, i, reads, done):
            flat = bounce.rearrange("j n m s -> j (n m s)")
            step = (NF + SHIFTS + 1) * QS
            for shift, n0, n1, row, chunk in reads:
                diagonal = flat[:, shift * QS:shift * QS + NF * step].rearrange("j (n x) -> n j x", x=step)
                eng.dma_start(zs_of(i)[row:row + n1 - n0, chunk, :].rearrange("n (j s) -> n j s", s=QS),
                              diagonal[n0:n1, :, 0:QS]).then_inc(done, 16)

        def is_early(i):
            return isinstance(i, int) and i < LAG

        def looks(i):
            return NL if is_early(i) else NT

        def before(i, early, later):
            return early * i if isinstance(i, int) and i <= LAG else early * LAG + later * (i - LAG)

        def looks_before(i):
            return before(i, NL, NT)

        def turned(i, g):
            return range(g * FPB, min(NG - NE * is_early(i), (g + 1) * FPB))

        early_home = [[h1_hi, h1_lo], [zs_hi, zs_lo]]

        def table_part(t, h):
            if t < NT:
                return table[:, t, h, :, :]
            return early_home[t - NT][h][:, :, :].rearrange("p o s -> p (o s)").rearrange("p (c d) -> p c d", d=P)

        def pairs_before(i):
            return before(i, -(-NL // 2), -(-NT // 2))

        ZU = TILES * UNITS // 2

        def last_in(i, t):
            return max(x for x in range(looks(i)) if x % BUFS == t % BUFS)

        block = ctx.enter_context(nc.Block())

        @block.sync
        def _(sp):
            def load_tile(i, k):
                t = TILES * i + k
                sp.dma_start(idx[:, k, :], ids_t[bass.ds(t, 1), :, :].rearrange("a p f -> p (a f)")
                             ).then_inc(idx_ready[k], 16)
                sp.dma_start(emb[:, k, 0, :], dense_t[bass.ds(t, 1), :, :].rearrange("a p d -> p (a d)")
                             ).then_inc(dense_ready[k], 16)

            for k in range(TILES):
                load_tile(0, k)
            sp.dma_start(ids_all, ids.rearrange("(t p) f -> p t f", p=P)).then_inc(ids_loaded, 16)
            sp.wait_ge(stage_zero, len(stage))
            for n, (kind, x) in enumerate(PIECES):
                if piece_before(n) is not None:
                    sp.wait_ge(piece_lo, piece_before(n) + 1)
                loaded, to = stage_loaded[STAGE_OF[n]], stage[STAGE_OF[n]]
                if kind == "table":
                    full = ROWS[x] // P
                    view = to.rearrange("p (c d) -> p c d", d=P)
                    sp.dma_start(view[:, 0:full, :], tables[(TABLED + EARLY)[x]][0:full * P, :].rearrange("(c p) d -> p c d", p=P)
                                 ).then_inc(loaded, 16)
                    if ROWS[x] > full * P:
                        sp.dma_start(view[0:ROWS[x] - full * P, full, :], tables[(TABLED + EARLY)[x]][full * P:ROWS[x], :]
                                     ).then_inc(loaded, 16)
                elif kind == "w2":
                    sp.dma_start(to.rearrange("p (c o) -> p c o", o=H2), w2.rearrange("(c p) o -> p c o", p=P)
                                 ).then_inc(loaded, 16)
                else:
                    sp.dma_start(to.rearrange("p (c o) -> p c o", o=H1), w1[:, x:x + WPC, :]
                                 ).then_inc(loaded, 16)

            sp.dma_start(w3s[:], w3).then_inc(small_loaded, 16)
            sp.dma_start(b2s[:], b2).then_inc(small_loaded, 16)

            def bounce_out(i, writes):
                for e in range(2):
                    sp.wait_ge(z_taken[e], ZU * i + ZU)
                    sp.sem_inc(sp_passed, 1)
                if not (isinstance(i, int) and i == 0):
                    sp.wait_ge(bounce_read, 16 * READS * i)
                    sp.sem_inc(sp_passed, 1)
                write_bounce(sp, writes, bounce_written)

            def bounce_in(i, reads):
                sp.wait_ge(bounce_written, written_before(i + 1))
                sp.sem_inc(sp_passed, 1)
                if i_is(i, PASSES - 1):
                    sp.wait_ge(pool_written, 16 * POOL_WRITES)
                if isinstance(i, int) and i == 0:
                    sp.wait_ge(bias_step, 1)
                elif i_is(i, PASSES - 1):
                    sp.wait_ge(bias_step, 2)
                else:
                    sp.wait_ge(zs_lo_made, i)
                read_bounce(sp, i, reads, bounce_read)

            def next_tile(i, k):
                sp.wait_ge(ring_full, fill_number(i, ("turn", k, TG - 1)) + 1)
                sp.sem_inc(sp_passed, 1)
                load_tile(i + 1, k)

            def one_pass(i):
                bounce_out(i - 1, WRITE)
                next_tile(i, 0)
                bounce_in(i - 1, READ)
                next_tile(i, 1)

            next_tile(0, 0)
            next_tile(0, 1)
            one_pass(1)
            with sp.Fori(LAG, PASSES - 1) as i:
                one_pass(i)
            bounce_out(PASSES - 2, WRITE)
            bounce_in(PASSES - 2, READ)
            bounce_out(PASSES - 1, WRITE[:-POOL_WRITES])
            bounce_in(PASSES - 1, READ[:-POOL_READS])
            sp.wait_ge(bounce_read, read_before(PASSES))
            sp.wait_ge(pool_read, 16 * POOL_READS)

        def piece_dmas(kind, x):
            return 2 if kind == "table" and ROWS[x] % P else 1

        def piece_loaded(n):
            return 16 * sum(piece_dmas(*PIECES[x]) for x in range(n + 1) if STAGE_OF[x] == STAGE_OF[n])

        def piece_split(kind, x):
            if kind == "table":
                return [table_part(x, h).rearrange("p c d -> p (c d)") for h in range(2)]
            if kind == "w2":
                return [w[:, :, :].rearrange("p c o -> p (c o)") for w in (w2_hi, w2_lo)]
            return [w[:, x:x + WPC, :].rearrange("p c o -> p (c o)") for w in (w1_hi, w1_lo)]

        @block.gpsimd
        def _(pool):
            def gather_tile(i, k):
                pool.wait_ge(idx_ready[k], 16 * i + 16)
                pool.sem_inc(tile_opened, 1)
                for g in range(TG):
                    for x in turned(i, g):
                        if x == 0:
                            continue
                        f = order[x] - 1
                        pool.indirect_dma_start(
                            emb[:, k, x, :], None, tables[f],
                            bass.IndirectOffsetOnAxis(ap=idx[:, k, f:f + 1].bitcast(U32), axis=0),
                        ).then_inc(gathered[k][g], 16)

            nc.gpsimd.memset(ident[:], 0.0).then_inc(consts_zero, 1)
            nc.gpsimd.memset(pick[:], 0.0).then_inc(consts_zero, 1)
            nc.gpsimd.iota(row_of_int[:], pattern=[[P, TC]], base=0, channel_multiplier=1).then_inc(consts_made, 1)
            pool.wait_ge(consts_zero, 2)
            nc.gpsimd.affine_select(out=ident[:], in_=ident[:], compare_op=ALU.not_equal, fill=1.0, base=0,
                                    pattern=[[-1, P]], channel_multiplier=1).then_inc(consts_made, 1)
            nc.gpsimd.affine_select(out=pick[:], in_=pick[:], compare_op=ALU.not_equal, fill=float(P), base=0,
                                    pattern=[[-1, NL]], channel_multiplier=1).then_inc(consts_zero, 1)
            pool.wait_ge(consts_zero, 3)
            nc.gpsimd.affine_select(out=pick[:], in_=pick[:], compare_op=ALU.not_equal, fill=1.0, base=-NL,
                                    pattern=[[-1, NL]], channel_multiplier=1).then_inc(consts_made, 1)
            for i in range(LAG):
                for k in range(TILES):
                    gather_tile(i, k)
            with pool.Fori(LAG, PASSES) as i:
                for k in range(TILES):
                    gather_tile(i, k)
            for e in range(2):
                pool.wait_ge(z_taken[e], ZU * PASSES)
            pool.wait_ge(bounce_read, 16 * READS * (PASSES - 1))
            write_bounce(pool, WRITE[-POOL_WRITES:], pool_written)
            pool.wait_ge(bounce_written, written_before(PASSES))
            pool.wait_ge(pool_written, 16 * POOL_WRITES)
            pool.wait_ge(bias_step, 2)
            read_bounce(pool, PASSES - 1, READ[-POOL_READS:], pool_read)

        def take_z(eng, copy, e, i, k, u):
            if k == 0 and u == e and not (isinstance(i, int) and i == 0):
                eng.wait_ge(bounce_written, 16 * WRITES * i)
            eng.wait_ge(z_full[e], ZU * i + (k * UNITS + u) // 2 + 1)
            s0 = k * GT + u * UNIT
            last = copy(zb[0:GROUP * NF, :, s0:s0 + UNIT],
                        zps[e][0:GROUP * NF, :, 0:GROUP * NF].rearrange("p g m -> p m g"))
            last.then_inc(z_taken[e], 1)

        @block.vector
        def _(dve):
            def make_onehot(i, t):
                dve.wait_ge(idb_full, pairs_before(i) + t // 2 + 1)
                if t >= BUFS:
                    dve.wait_ge(ring_full, fill_number(i, ("look", t - BUFS)) + 1)
                elif not i_is(i, 0):
                    dve.wait_ge(ring_full, fill_number(i - 1, ("look", last_in(i - 1, t))) + 1)
                nc.vector.tensor_tensor(
                    onehot[:, t % BUFS, :, :],
                    idb[:, t % 2, :].unsqueeze(1).to_broadcast([P, TC, NS]),
                    row_of[:].unsqueeze(2).to_broadcast([P, TC, NS]),
                    ALU.is_equal).then_inc(onehot_made, 1)

            def split_h1(i, x):
                n = 2 * (i - LAG) + x + 1
                dve.wait_ge(h1_hi_made, n)
                nc.vector.scalar_tensor_tensor(
                    out=h1_lo[:, 2 * x:2 * x + 2, :].rearrange("p o s -> p (o s)"), in0=ring[bank(i, ("l1", x))][:],
                    scalar=0.0, in1=h1_hi[:, 2 * x:2 * x + 2, :].rearrange("p o s -> p (o s)").bitcast(F32),
                    op0=ALU.max, op1=ALU.subtract).then_inc(h1_lo_made, 1)

            def place_dense(i):
                dve.wait_ge(ring_taken, fill_number(i, ("turn", 1, TG - 1)) + 1)
                if not i_is(i, 0) and not i_is(i, PASSES - 1):
                    dve.wait_ge(zs_lo_made, i)
                for k in range(TILES):
                    nc.vector.tensor_copy(zs_of(i)[:, ZC, :].rearrange("p (j k g) -> p k j g", j=GROUP, k=TILES)[:, k],
                                          xt[:, k, :, 0].rearrange("p (g j) -> p j g", j=GROUP)
                                          ).then_inc(dense_placed, 1)

            def split_zs(i):
                dve.wait_ge(zs_hi_made, i)
                nc.vector.tensor_tensor(zs_lo[:], zs_of(i - 1)[:, :, :], zs_hi[:].bitcast(F32), ALU.subtract).then_inc(zs_lo_made, 1)

            def piece_to_lo(n):
                hi, lo = piece_split(*PIECES[n])
                dve.wait_ge(piece_hi, n + 1)
                nc.vector.tensor_tensor(lo, stage[STAGE_OF[n]], hi.bitcast(F32), ALU.subtract).then_inc(piece_lo, 1)

            def one_pass(i, mlp, last):
                for t in range(BUFS, looks(i)):
                    make_onehot(i, t)
                    if i_is(i, 0) and NT + t - BUFS < NL:
                        piece_to_lo(NT + t - BUFS)
                if i_is(i, 0):
                    for n in range(NL, len(PIECES)):
                        piece_to_lo(n)
                    dve.wait_ge(piece_lo, len(PIECES))
                    nc.vector.memset(zs[:], 1.0).then_inc(bias_step, 1)
                    dve.wait_ge(bias_step, 1)
                if not last:
                    if mlp:
                        split_h1(i, 0)
                    make_onehot(i + 1, 0)
                    make_onehot(i + 1, 1)
                take_z(dve, nc.vector.tensor_copy, 0, i, 0, 0)
                if not last:
                    make_onehot(i + 1, 2)
                    if mlp:
                        split_h1(i, 1)
                take_z(dve, nc.vector.tensor_copy, 0, i, 0, 2)
                if not last:
                    make_onehot(i + 1, 3)
                    if not i_is(i, 0):
                        split_zs(i)
                    place_dense(i)
                take_z(dve, nc.vector.tensor_copy, 0, i, 1, 0)
                take_z(dve, nc.vector.tensor_copy, 0, i, 1, 2)
                if last:
                    dve.wait_ge(ring_full, fill_number(i, ("turn", 0, TG - 1)) + 1)
                    nc.vector.memset(late_zs, 1.0).then_inc(bias_step, 1)
                    dve.wait_ge(bias_step, 2)
                    place_dense(i)

            for piece in stage:
                nc.vector.memset(piece[:, min(ROWS) // P * P:], 0.0).then_inc(stage_zero, 1)
            dve.wait_ge(ids_loaded, 16)
            for n, f in enumerate(TABLED + EARLY):
                nc.vector.tensor_scalar(halves_int[:, :, n], ids_all[:, :, f], LOG_P, None,
                                        ALU.logical_shift_right).then_inc(halves_step, 1)
                nc.vector.tensor_scalar(halves_int[:, :, NL + n], ids_all[:, :, f], P - 1, None,
                                        ALU.bitwise_and).then_inc(halves_step, 1)
            dve.wait_ge(halves_step, 2 * NL)
            nc.vector.tensor_copy(halves, halves_int).then_inc(halves_step, 1)
            dve.wait_ge(consts_made, 3)
            nc.vector.tensor_copy(row_of[:], row_of_int[:]).then_inc(halves_step, 1)
            dve.wait_ge(halves_step, 2 * NL + 2)
            for n in range(NT):
                piece_to_lo(n)
                if n == 0 or n % 2 == 1:
                    make_onehot(0, (n + 1) // 2)
            one_pass(0, mlp=False, last=False)
            one_pass(1, mlp=False, last=False)
            with dve.Fori(LAG, PASSES - 1) as i:
                one_pass(i, mlp=True, last=False)
            one_pass(PASSES - 1, mlp=True, last=True)
            for i, what in TAIL:
                if what[0] == "l1":
                    split_h1(i, what[1])
                if what == LAST[1] and i <= PASSES:
                    split_zs(i)

        @block.scalar
        def _(act):
            def take_turn(i, k, g):
                what = ("turn", k, g)
                fs = turned(i, g)
                act.wait_ge(ring_full, fill_number(i, what) + 1)
                if g == 0 and not i_is(i, 0):
                    act.wait_ge(dense_placed, TILES * i)
                nc.scalar.copy(xt[:, k, :, fs[0]:fs[-1] + 1],
                               ring[bank(i, what)][:, 0:len(fs) * P].rearrange("p (f s) -> p s f", f=len(fs))
                               ).then_inc(ring_taken, 1)

            def take_turns(i, k, gs=range(TG)):
                for g in gs:
                    take_turn(i, k, g)

            def take_look(i, t):
                what = ("look", t)
                act.wait_ge(ring_full, fill_number(i, what) + 1)
                at = NG + t if t < NT else NG - NE + t - NT
                nc.scalar.copy(xt[:, :, :, at], ring[bank(i, what)][:, 0:NS].rearrange("p (k s) -> p k s", k=TILES)
                               ).then_inc(ring_taken, 1)

            def take_l1(i, x):
                what = ("l1", x)
                act.wait_ge(ring_full, fill_number(i, what) + 1)
                nc.scalar.activation(h1_hi[:, 2 * x:2 * x + 2, :].rearrange("p o s -> p (o s)"),
                                     ring[bank(i, what)][:], ACT.Relu).then_inc(h1_hi_made, 1)
                act.wait_ge(h1_lo_made, 2 * (i - LAG) + x + 1)
                act.sem_inc(ring_taken, 1)

            def take_l2(i):
                what = ("l2",)
                act.wait_ge(ring_full, fill_number(i, what) + 1)
                act.wait_ge(yrow_free, 16 * (i - LAG) + 16)
                for o in range(O2):
                    last = nc.scalar.activation(h2[:, o, :], ring[bank(i, what)][:, o * NS:(o + 1) * NS], ACT.Relu,
                                                bias=b2s[:, o:o + 1])
                last.then_inc(ring_taken, 1)

            def take_l3(i):
                what = ("l3",)
                act.wait_ge(ring_full, fill_number(i, what) + 1)
                n = i - LAG
                nc.scalar.copy(yrow.rearrange("o (k g j) -> o j k g", k=TILES, j=GROUP),
                               ring[bank(i, what)][0:1, 0:NS].rearrange("o (j k g) -> o j k g", k=TILES, j=GROUP)
                               ).then_inc(ring_taken, 1)
                act.wait_ge(ring_taken, fill_number(i, what) + 1)
                act.dma_start(out_row[:, bass.ds(NS * n, NS)], yrow).then_inc(yrow_free, 16)

            def split_zs(i):
                act.wait_ge(bounce_read, read_before(i))
                if i_is(i, PASSES):
                    act.wait_ge(pool_read, 16 * POOL_READS)
                act.wait_ge(dense_placed, TILES * i)
                nc.scalar.copy(zs_hi[:], zs_of(i - 1)[:, :, :]).then_inc(zs_hi_made, 1)

            def piece_to_hi(n):
                act.wait_ge(stage_loaded[STAGE_OF[n]], piece_loaded(n))
                nc.scalar.copy(piece_split(*PIECES[n])[0], stage[STAGE_OF[n]]).then_inc(piece_hi, 1)

            def take_mlp(i, what):
                if what[0] == "l1":
                    take_l1(i, what[1])
                elif what[0] == "l2":
                    take_l2(i)
                else:
                    take_l3(i)

            def one_pass(i, mlp, last=False):
                if not i_is(i, 0):
                    take_turns(i, 0, range(RING))
                for t in range(looks(i)):
                    take_look(i, t)
                    if i_is(i, 0) and t == FIRST_LOOKS - 1:
                        take_turns(i, 0)
                    if not i_is(i, 0) and t == 0:
                        take_turns(i, 0, range(RING, TG))
                    if mlp and not last and t == BUFS - 1:
                        take_l1(i, 0)
                    if i_is(i, 0) and NL + t < len(PIECES):
                        piece_to_hi(NL + t)
                if not last:
                    take_turns(i, 1, range(RING))
                if i_is(i, 0):
                    act.wait_ge(bias_step, 1)
                take_z(act, nc.scalar.copy, 1, i, 0, 1)
                if not last:
                    take_turns(i, 1, range(RING, TG))
                if mlp and not last:
                    take_l1(i, 1)
                take_z(act, nc.scalar.copy, 1, i, 0, 3)
                if last:
                    take_turns(i, 1)
                elif not i_is(i, 0):
                    split_zs(i)
                if mlp and not last:
                    take_l2(i)
                take_z(act, nc.scalar.copy, 1, i, 1, 1)
                if mlp and not last:
                    take_l3(i)
                take_z(act, nc.scalar.copy, 1, i, 1, 3)

            for e in range(2):
                w = UNIT * P
                act.wait_ge(ids_turned_full, e + 1)
                nc.scalar.copy(ids_turned[:, e * w:(e + 1) * w], zps[e][0:2 * NL, :, :].rearrange("p t s -> p (t s)")
                               ).then_inc(ids_turned_taken, 1)
                if e == 0:
                    piece_to_hi(0)
                    piece_to_hi(1)
            for n in range(2, NL):
                piece_to_hi(n)
            act.sem_inc(yrow_free, 16)

            one_pass(0, mlp=False)
            one_pass(1, mlp=False)
            act.wait_ge(small_loaded, 32)
            with act.Fori(LAG, PASSES - 1) as i:
                one_pass(i, mlp=True)
            one_pass(PASSES - 1, mlp=True, last=True)
            for i, what in TAIL:
                take_mlp(i, what)
                if what == LAST[1] and i <= PASSES:
                    split_zs(i)
            act.wait_ge(yrow_free, 16 * PASSES + 16)

        @block.tensor
        def _(pe):
            def open_bank(i, what):
                n = fill_number(i, what)
                if not isinstance(n, int) or n >= RING:
                    pe.wait_ge(ring_taken, n - RING + 1)
                return ring[bank(i, what)]

            def turn(i, k, g):
                ps = open_bank(i, ("turn", k, g))
                per_pass = [len([x for x in turned(j, g) if x > 0]) for j in (0, LAG)]
                pe.wait_ge(gathered[k][g], 16 * before(i + 1, *per_pass))
                if g == 0:
                    pe.wait_ge(dense_ready[k], 16 * i + 16)
                for x, f in enumerate(turned(i, g)):
                    last = nc.tensor.transpose(ps[:, x * P:(x + 1) * P], emb[:, k, f, :], ident[:])
                last.then_inc(ring_full, 1)

            def broadcast_ids(i, pair):
                done = looks_before(i) + 2 * pair
                if not isinstance(done, int) or done > 0:
                    pe.wait_ge(onehot_made, done)
                    pe.sem_inc(idb_opened, 1)
                for t in range(2 * pair, min(looks(i), 2 * pair + 2)):
                    last = nc.tensor.matmul(idb[:, t % 2, :], pick[:, t:t + 1].to_broadcast([2 * NL, P]), ids_turned[:, bass.ds(i * NS, NS)],
                                            start=True, stop=True)
                last.then_inc(idb_full, 1)

            def look_up(i, t):
                ps = open_bank(i, ("look", t))
                pe.wait_ge(onehot_made, looks_before(i) + t + 1)
                for c in range(TC):
                    kk = min(P, ROWS[t] - c * P)
                    for h in range(2):
                        last = nc.tensor.matmul(ps[:, 0:NS], table_part(t, h)[0:kk, c, :], onehot[0:kk, t % BUFS, c, :],
                                                start=(c == 0 and h == 0), stop=(c == TC - 1 and h == 1))
                last.then_inc(ring_full, 1)

            def products(i, k, u):
                e, nth = u % 2, (k * UNITS + u) // 2
                if not (isinstance(i, int) and i == 0 and nth == 0):
                    pe.wait_ge(z_taken[e], ZU * i + nth)
                for g in range(UNIT):
                    s = (u * UNIT + g) * GROUP
                    last = nc.tensor.matmul(
                        zps[e][0:GROUP * NF, g, 0:GROUP * NF], xt[:, k, s:s + GROUP, :].rearrange("p s f -> p (s f)"),
                        xt[:, k, s:s + GROUP, :].rearrange("p s f -> p (s f)"), start=True, stop=True)
                last.then_inc(z_full[e], 1)

            def split_product(ps, w_hi, w_lo, x_hi, x_lo, first, last_one):
                nc.tensor.matmul(ps, w_hi, x_hi, start=first, stop=False)
                nc.tensor.matmul(ps, w_hi, x_lo, start=False, stop=False)
                return nc.tensor.matmul(ps, w_lo, x_hi, start=False, stop=last_one)

            def layer1(i, x):
                ps = open_bank(i, ("l1", x))
                pe.wait_ge(zs_lo_made, i - LAG + 1)
                for o in range(2 * x, 2 * x + 2):
                    for c in range(C1):
                        kk = ZR + 1 if c == 0 else ZR if c < ZC else P
                        cols = slice(o * P, (o + 1) * P)
                        last = split_product(ps[:, (o % 2) * NS:(o % 2 + 1) * NS], w1_hi[0:kk, c, cols],
                                             w1_lo[0:kk, c, cols], zs_hi[0:kk, c, :], zs_lo[0:kk, c, :],
                                             c == 0, c == C1 - 1)
                last.then_inc(ring_full, 1)

            def layer2(i):
                ps = open_bank(i, ("l2",))
                for o in range(O2):
                    for c in range(O1):
                        if o == 0 and c % 2 == 0:
                            pe.wait_ge(h1_lo_made, 2 * (i - LAG) + c // 2 + 1)
                            pe.sem_inc(h1_opened, 1)
                        cols = slice(o * P, (o + 1) * P)
                        last = split_product(ps[:, o * NS:(o + 1) * NS], w2_hi[:, c, cols], w2_lo[:, c, cols],
                                             h1_hi[:, c, :], h1_lo[:, c, :], c == 0, c == O1 - 1)
                last.then_inc(ring_full, 1)

            def layer3(i):
                ps = open_bank(i, ("l3",))
                pe.wait_ge(ring_taken, fill_number(i, ("l2",)) + 1)
                for c in range(O2):
                    last = nc.tensor.matmul(ps[0:1, 0:NS], w3s[:, c:c + 1], h2[:, c, :],
                                            start=(c == 0), stop=(c == O2 - 1))
                last.then_inc(ring_full, 1)

            def layer(i, what):
                if what[0] == "l1":
                    layer1(i, what[1])
                elif what[0] == "l2":
                    layer2(i)
                else:
                    layer3(i)

            def one_pass(i, mlp, last):
                if not i_is(i, 0):
                    for g in range(RING):
                        turn(i, 0, g)
                for t in range(looks(i)):
                    look_up(i, t)
                    if not i_is(i, 0) and t == 0:
                        for g in range(RING, TG):
                            turn(i, 0, g)
                    if i_is(i, 0) and t == FIRST_LOOKS - 1:
                        for g in range(TG):
                            turn(i, 0, g)
                    if i_is(i, 0) and t % 2 == 0 and t + 2 < NL:
                        broadcast_ids(i, t // 2 + 1)
                    if not i_is(i, 0) and t % 2 == 1 and BUFS - 1 <= t < looks(i) - 3:
                        broadcast_ids(i, (t + 3) // 2)
                    if mlp and not last and t == BUFS - 1:
                        layer(i, ("l1", 0))
                if not last:
                    broadcast_ids(i + 1, 0)
                if not last:
                    for g in range(RING):
                        turn(i, 1, g)
                pe.wait_ge(ring_taken, fill_number(i, ("look", looks(i) - 1)) + 1)
                products(i, 0, 0)
                products(i, 0, 1)
                if not last:
                    for g in range(RING, TG):
                        turn(i, 1, g)
                if not last:
                    broadcast_ids(i + 1, 1)
                if mlp and not last:
                    layer(i, ("l1", 1))
                products(i, 0, 2)
                products(i, 0, 3)
                if mlp and not last:
                    layer(i, ("l2",))
                if last:
                    for g in range(TG):
                        turn(i, 1, g)
                pe.wait_ge(ring_taken, fill_number(i, ("turn", 1, TG - 1)) + 1)
                products(i, 1, 0)
                products(i, 1, 1)
                if not last:
                    broadcast_ids(i + 1, 2)
                    if mlp:
                        layer(i, ("l3",))
                products(i, 1, 2)
                products(i, 1, 3)

            pe.wait_ge(consts_made, 3)
            pe.wait_ge(halves_step, 2 * NL + 2)
            for e in range(2):
                for t in range(UNIT):
                    last = nc.tensor.transpose(zps[e][0:2 * NL, t, :], halves[:, e * UNIT + t, :], ident[:])
                last.then_inc(ids_turned_full, 1)
                if e == 0:
                    pe.wait_ge(ids_turned_taken, 1)
                    broadcast_ids(0, 0)
            pe.wait_ge(ids_turned_taken, 2)

            one_pass(0, mlp=False, last=False)
            one_pass(1, mlp=False, last=False)
            with pe.Fori(LAG, PASSES - 1) as i:
                one_pass(i, mlp=True, last=False)
            one_pass(PASSES - 1, mlp=True, last=True)
            for i, what in TAIL:
                layer(i, what)


def kernel(**inputs):
    import numpy as np
    import concourse.bacc as bacc
    from concourse.bass_utils import run_bass_kernel_spmd

    nc = bacc.Bacc("TRN2", target_bir_lowering=False, num_devices=1, dynamic_dma_scratch_size=8192)
    arrays = {}

    def dram(name, a):
        arrays[name] = np.ascontiguousarray(a)
        return nc.dram_tensor(name, arrays[name].shape, mybir.dt.from_np(arrays[name].dtype),
                              kind="ExternalInput").ap()

    ids = inputs["ids"]
    n = ids.shape[1] + 1
    order = feature_order(n - 1)
    w1 = np.asarray(inputs["W_top1"])
    pairs = n * (n - 1) // 2
    chunks = 3
    per = pairs // chunks
    w1_chunks = np.zeros((P, chunks + 1, w1.shape[1]), w1.dtype)
    for row in range(pairs):
        shift, a = row // n + 1, row % n
        b = (a + shift) % n
        lo, hi = min(order[a], order[b]), max(order[a], order[b])
        w1_chunks[row % per, row // per] = w1[lo * n - lo * (lo + 1) // 2 + hi - lo - 1]
    w1_chunks[per, 0] = np.asarray(inputs["b_top1"])
    w1_chunks[:, chunks] = w1[pairs:]
    args = dict(
        dense=dram("dense", inputs["r_dense"]), ids=dram("ids", ids),
        tables=[dram(f"tbl_{f}", inputs[f"tbl_{f}"]) for f in range(n - 1)],
        w1=dram("w1", w1_chunks),
        w2=dram("w2", inputs["W_top2"]),
        b2=dram("b2", np.asarray(inputs["b_top2"]).reshape(-1, P).T),
        w3=dram("w3", np.asarray(inputs["W_top3"]).reshape(-1, P).T),
    )
    out = nc.dram_tensor("scores", (ids.shape[0], 1), F32, kind="ExternalOutput").ap()
    dlrm_tower(nc, out=out, **args)
    r = run_bass_kernel_spmd(nc, [arrays], core_ids=[0])
    return r.results[0]["scores"]
```
